# Optimizing a Trainium2 kernel written in Bass

```python
import numpy as np
import jax
import jax.numpy as jnp

def _softmax(x, axis=-1):
    return jax.nn.softmax(x, axis=axis)

def _gelu(x):
    return jax.nn.gelu(x, approximate=True)

def _silu(x):
    return jax.nn.silu(x)

def _sigmoid(x):
    return jax.nn.sigmoid(x)

def _layernorm(x, axis=-1, eps=1e-05):
    m = jnp.mean(x, axis=axis, keepdims=True)
    v = jnp.var(x, axis=axis, keepdims=True)
    return (x - m) / jnp.sqrt(v + eps)

def _scatter_add(tgt, idx, src, axis=0):
    return tgt.at[idx].add(src)

def _segment_sum(src, seg, n):
    return jax.ops.segment_sum(src, seg, n)
kernel_name = 'mk_cond_resid_d2_seqx_r2_f672d7'

def setup_inputs(seed: int=0):
    np.random.seed(seed)
    _w = jnp.asarray

    def _rec_inputs():
        import jax
        import jax.numpy as jnp
        _rk = jax.random.key(seed)
        x = -0.000125 + 0.9999 * jax.random.normal(jax.random.fold_in(_rk, 1), (16, 512, 512), jnp.float32)
        _lenS = 512 - jax.random.randint(jax.random.fold_in(_rk, 7), (16,), 0, max(1, 512 // 4) + 1, jnp.int32)
        _lenS2 = 512 - jax.random.randint(jax.random.fold_in(_rk, 8), (16,), 0, max(1, 512 // 4) + 1, jnp.int32)
        cond_1024 = -0.00493535 + 1.00056 * jax.random.normal(jax.random.fold_in(_rk, 11), (16, 512), jnp.float32)
        return (x, cond_1024)
    x, cond_1024 = _rec_inputs()

    def _L0_cond_setup():
        import jax, jax.numpy as jnp
        import numpy as np
        import math
        N, T, D, H = (64, 256, 512, 512)
        key = jax.random.key(seed)
        k1, k2, k3, k4 = jax.random.split(key, 4)
        x = jax.random.normal(k1, (N, T, D), dtype=jnp.float32)
        h0 = jax.random.normal(k2, (N, H), dtype=jnp.float32)
        Wx = jax.random.normal(k3, (D, 4 * H), dtype=jnp.float32) / math.sqrt(D)
        Wh = jax.random.normal(k4, (H, 4 * H), dtype=jnp.float32) / math.sqrt(H)
        b = jnp.zeros((4 * H,), dtype=jnp.float32)
        return {'x': x, 'h0': h0, 'Wx': Wx, 'Wh': Wh, 'b': b}
    _L0_cond_all = _L0_cond_setup()
    _L0_cond_in = {k: v for k, v in _L0_cond_all.items() if k in ('Wx', 'Wh', 'b')}
    del _L0_cond_all

    def _L1_cond_setup():
        import jax, jax.numpy as jnp
        import numpy as np
        N, T, D, H = (128, 256, 512, 512)
        key = jax.random.key(seed)
        k1, k2, k3, k4 = jax.random.split(key, 4)
        x = jax.random.normal(k1, (N, T, D), dtype=jnp.float32)
        h0 = jax.random.normal(k2, (N, H), dtype=jnp.float32)
        Wx = jax.random.normal(k3, (D, H), dtype=jnp.float32) / np.sqrt(D)
        Wh = jax.random.normal(k4, (H, H), dtype=jnp.float32) / np.sqrt(H)
        b = jnp.zeros((H,), dtype=jnp.float32)
        return {'x': x, 'h0': h0, 'Wx': Wx, 'Wh': Wh, 'b': b}
    _L1_cond_all = _L1_cond_setup()
    _L1_cond_in = {k: v for k, v in _L1_cond_all.items() if k in ('Wx', 'Wh', 'b')}
    del _L1_cond_all
    return {'x': x, 'cond_1024': cond_1024, 'L0_cond_Wx': _L0_cond_in['Wx'], 'L0_cond_Wh': _L0_cond_in['Wh'], 'L0_cond_b': _L0_cond_in['b'], 'L1_cond_Wx': _L1_cond_in['Wx'], 'L1_cond_Wh': _L1_cond_in['Wh'], 'L1_cond_b': _L1_cond_in['b']}

def reference(x, cond_1024, L0_cond_Wx, L0_cond_Wh, L0_cond_b, L1_cond_Wx, L1_cond_Wh, L1_cond_b):
    import jax
    import jax.numpy as jnp

    def _L0_cond_ref(x, h0, Wx, Wh, b):
        import jax, jax.numpy as jnp
        import numpy as np
        import math
        N, T, D, H = (64, 256, 512, 512)
        Hdim = h0.shape[1]
        c0 = jnp.zeros_like(h0)
        xW = jnp.einsum('ntd,dk->tnk', x, Wx) + b

        def step(carry, xw_t):
            prev_h, prev_c = carry
            a = xw_t + prev_h @ Wh
            i = jax.nn.sigmoid(a[:, :Hdim])
            f = jax.nn.sigmoid(a[:, Hdim:2 * Hdim])
            o = jax.nn.sigmoid(a[:, 2 * Hdim:3 * Hdim])
            g = jnp.tanh(a[:, 3 * Hdim:])
            next_c = f * prev_c + i * g
            next_h = o * jnp.tanh(next_c)
            return ((next_h, next_c), next_h)
        _, hs = jax.lax.scan(step, (h0, c0), xW)
        return jnp.transpose(hs, (1, 0, 2))

    def _L1_cond_ref(x, h0, Wx, Wh, b):
        import jax, jax.numpy as jnp
        import numpy as np
        N, T, D, H = (128, 256, 512, 512)
        xW = jnp.einsum('ntd,dh->tnh', x, Wx) + b

        def step(h, xw_t):
            h_next = jnp.tanh(h @ Wh + xw_t)
            return (h_next, h_next)
        _, hs = jax.lax.scan(step, h0, xW)
        return jnp.swapaxes(hs, 0, 1)
    x = x + _L0_cond_ref(x, cond_1024, L0_cond_Wx, L0_cond_Wh, L0_cond_b)
    x = x + _L1_cond_ref(x, cond_1024, L1_cond_Wx, L1_cond_Wh, L1_cond_b)
    return x

_drawn_inputs = setup_inputs


def setup_inputs(seed=0):
    import zlib

    import numpy as np

    out = dict(_drawn_inputs(seed))
    spreads = {'L0_cond_b': (0.0, 0.1), 'L1_cond_b': (0.0, 0.1)}
    factors = {}
    for name, (base, spread) in spreads.items():
        noise = np.random.default_rng([zlib.crc32(name.encode()), seed]).standard_normal(out[name].shape)
        drawn = base * np.exp(spread * noise) if base else spread * noise
        out[name] = jnp.asarray(drawn.astype(out[name].dtype))
    for name, factor in factors.items():
        out[name] = (out[name] * factor).astype(out[name].dtype)
    return out
```

```python
from contextlib import ExitStack

import numpy as np

import concourse.bass as bass
from concourse import mybir

BATCH, STEPS, DIM = 16, 512, 512
P = 128
SUB = DIM // P
QUADS, QUAD = 4, 32
GATES = 4
GATE_ORDER = [0, 1, 3, 2]
BLOCKS = GATES * SUB
CHUNK = 16
GROUP = 8
LAG = 2 * GROUP
BODY = 2 * CHUNK
CHUNKS = STEPS // CHUNK
GROUPS = STEPS // GROUP
BLOCKS_PER_STEP = BLOCKS // CHUNK
H_SCALE = 2.0 ** 15
SIG = (GATES - 1) * SUB * BATCH
CELL = SUB * BATCH

fp32, fp16, i32 = mybir.dt.float32, mybir.dt.float16, mybir.dt.int32
ALU = mybir.AluOpType
ACT = mybir.ActivationFunctionType


def residual_lstm_rnn(nc, xT, h0T, wx0, wh0, b0, wx1, wh1, b1, yT):
    with ExitStack() as ctx:
        def sb(name, shape, dt=fp32):
            return ctx.enter_context(nc.sbuf_tensor(name, shape, dt))

        def pb(name):
            return ctx.enter_context(nc.psum_tensor(name, [P, 512], fp32))

        def sem(name):
            return ctx.enter_context(nc.semaphore(name))

        wx0_sb = sb("wx0_sb", [P, SUB, BLOCKS, P])
        wh0_sb = sb("wh0_sb", [P, SUB, BLOCKS, P])
        wx1_sb = sb("wx1_sb", [P, SUB, SUB, P])
        wh1_sb = sb("wh1_sb", [P, SUB, SUB, P])
        wh0_part = [sb(f"wh0_part{i}", [P, SUB, QUADS, BLOCKS * QUAD], fp16) for i in range(2)]
        wh1_part = [sb(f"wh1_part{i}", [P, SUB, QUADS, SUB * QUAD], fp16) for i in range(2)]
        b0_sb = sb("b0_sb", [P, BLOCKS])
        b1_sb = sb("b1_sb", [P, SUB])
        largest = [sb(f"largest{l}", [P, 1]) for l in range(2)]
        largest_all = [sb(f"largest_all{l}", [P, 1]) for l in range(2)]
        power = [sb(f"power{l}", [P, 1]) for l in range(2)]
        w_scale = [sb(f"w_scale{l}", [P, 1]) for l in range(2)]
        w_scale_half = sb("w_scale_half", [P, 1])
        unscale = [sb(f"unscale{l}", [P, 1]) for l in range(2)]
        h_first = sb("h_first", [P, SUB, 2 * BATCH])
        h0_parts = sb("h0_parts", [P, SUB, 2 * BATCH], fp16)
        h1_parts = sb("h1_parts", [P, SUB, 2 * BATCH], fp16)
        x_bulk = sb("x_bulk", [P, 2, SUB, CHUNK * BATCH])
        x_res = sb("x_res", [P, 2, SUB, CHUNK, BATCH])
        xw0 = sb("xw0", [P, 2, CHUNK, BLOCKS * BATCH])
        y0 = sb("y0", [P, 2, SUB, GROUP, BATCH])
        xw1 = sb("xw1", [P, 2, GROUP, CELL])
        y1 = sb("y1", [P, 2, SUB, GROUP, BATCH])
        turned0 = sb("turned0", [P, BLOCKS, 2 * BATCH])
        sum0 = sb("sum0", [P, BLOCKS * BATCH])
        pre0 = sb("pre0", [P, BLOCKS * BATCH])
        ifgc = sb("ifgc", [P, 4, CELL])
        o_t = sb("o_t", [P, CELL])
        uv = sb("uv", [P, 2, CELL])
        o_scaled = sb("o_scaled", [P, CELL])
        tanh_c = sb("tanh_c", [P, CELL])
        h0_full = sb("h0_full", [P, CELL])
        turned1 = sb("turned1", [P, SUB, 2 * BATCH])
        sum1 = sb("sum1", [P, CELL])
        pre1 = sb("pre1", [P, CELL])
        h1_full = sb("h1_full", [P, CELL])

        rec0_ps, rec1_ps = pb("rec0_ps"), pb("rec1_ps")
        bulk0_ps = [pb(f"bulk0_ps{i}") for i in range(2)]
        bulk1_ps = [pb(f"bulk1_ps{i}") for i in range(2)]

        wx0_in = [sem(f"wx0_in{k}") for k in range(SUB)]
        wh0_in, wh1_in, wx1_in, b_in, h_in = (sem(n) for n in ("wh0_in", "wh1_in", "wx1_in", "b_in", "h_in"))
        h_zeroed, cell_zeroed, b0_halved = sem("h_zeroed"), sem("cell_zeroed"), sem("b0_halved")
        prep, largest_done, reduced = sem("prep"), sem("largest_done"), sem("reduced")
        scaled, w_high, w_low = sem("scaled"), sem("w_high"), sem("w_low")
        x_bulk_in = [sem(f"x_bulk_in{i}") for i in range(2)]
        x_res_in = [sem(f"x_res_in{i}") for i in range(2)]
        y1_out = [sem(f"y1_out{i}") for i in range(2)]
        rec0_done, turned_ifg, turned_o = sem("rec0_done"), sem("turned_ifg"), sem("turned_o")
        sum_ifg, pre_ifg, sum_o, pre_o = sem("sum_ifg"), sem("pre_ifg"), sem("sum_o"), sem("pre_o")
        ifg_done, o_done, uv_done, cell_done = sem("ifg_done"), sem("o_done"), sem("uv_done"), sem("cell_done")
        tanh_c_done, o_scaled_done = sem("tanh_c_done"), sem("o_scaled_done")
        h0_full_done, h0_high, h0_ready = sem("h0_full_done"), sem("h0_high"), sem("h0_ready")
        y0_done = sem("y0_done")
        bulk0_done, xw0_done = sem("bulk0_done"), sem("xw0_done")
        bulk1_done, xw1_done = sem("bulk1_done"), sem("xw1_done")
        rec1_done, turned1_done, sum1_done, pre1_done = (
            sem("rec1_done"), sem("turned1_done"), sem("sum1_done"), sem("pre1_done"))
        h1_full_done, h1_high, h1_ready, y1_done = (
            sem("h1_full_done"), sem("h1_high"), sem("h1_ready"), sem("y1_done"))

        def phases(eng, steps):
            steps(0, 0, BODY)
            with eng.Fori(1, STEPS // BODY - 1) as i:
                steps(i, BODY, BODY)
            steps(STEPS // BODY - 1, STEPS - BODY, BODY)
            steps(STEPS // BODY, STEPS, LAG)

        def loads(i, j, ahead):
            return i * 16 + 16 * ((j // CHUNK + ahead) // 2 + 1)

        def w_pieces():
            return ([(0, k, q, lo, hi) for k in range(SUB) for q in range(QUADS)
                     for lo, hi in ((0, 2 * SUB), (2 * SUB, 3 * SUB), (3 * SUB, BLOCKS))]
                    + [(1, k, q, 0, SUB) for k in range(SUB) for q in range(QUADS)])

        def w_piece(l, k, q, lo, hi):
            w_sb, parts = ((wh0_sb, wh0_part), (wh1_sb, wh1_part))[l]
            w32 = w_sb[:, k, lo:hi, QUAD * q:QUAD * (q + 1)]
            high, low = (h[:, k, q].rearrange("p (b c) -> p b c", c=QUAD)[:, lo:hi] for h in parts)
            halved = l == 0 and lo != 2 * SUB
            return w32, high, low, (w_scale_half if halved else w_scale[l])[:, :]


        block = ctx.enter_context(nc.Block())

        @block.sync
        def _(sp):
            for k in range(SUB):
                sp.dma_start(wx0_sb[:, k], wx0[:, k]).then_inc(wx0_in[k], 16)
                if k == 0:
                    sp.dma_start(x_bulk[:, 0], xT[0].rearrange("p s t n -> p s (t n)")).then_inc(x_bulk_in[0], 16)
                    sp.dma_start(b0_sb[:, :], b0).then_inc(b_in, 16)
                    sp.dma_start(b1_sb[:, :], b1).then_inc(b_in, 16)
            sp.dma_start(wh0_sb[:, :], wh0).then_inc(wh0_in, 16)
            sp.dma_start(wh1_sb[:, :], wh1).then_inc(wh1_in, 16)
            sp.wait_ge(h_zeroed, 1)
            sp.dma_start(h_first[:, :, 0:BATCH], h0T).then_inc(h_in, 16)
            sp.dma_start(x_res[:, 0], xT[0]).then_inc(x_res_in[0], 16)
            sp.dma_start(x_bulk[:, 1], xT[1].rearrange("p s t n -> p s (t n)")).then_inc(x_bulk_in[1], 16)
            sp.dma_start(wx1_sb[:, :], wx1).then_inc(wx1_in, 16)

            def steps(i, at, count):
                for j in range(0, count, GROUP):
                    t, a = i * BODY + j, at + j
                    v = a // CHUNK
                    if a % CHUNK == 0 and v + 1 < CHUNKS:
                        if a:
                            sp.wait_ge(y0_done, t)
                        chunk = i * (BODY // CHUNK) + j // CHUNK
                        sp.dma_start(x_res[:, (v + 1) % 2], xT[bass.ds(chunk + 1, 1)].rearrange("a p s t n -> (a p) s t n")
                                     ).then_inc(x_res_in[(v + 1) % 2], 16)
                        if v + 2 < CHUNKS:
                            sp.wait_ge(bulk0_done, t * BLOCKS_PER_STEP + BLOCKS)
                            sp.dma_start(x_bulk[:, v % 2], xT[bass.ds(chunk + 2, 1)].rearrange("a p s t n -> (a p) s (t n)")
                                         ).then_inc(x_bulk_in[v % 2], 16)
                    if a >= LAG + GROUP:
                        slot = a // GROUP % 2 ^ 1
                        sp.wait_ge(y1_done, t - LAG)
                        group = i * (BODY // GROUP) + ((j - LAG) // GROUP - 1)
                        sp.dma_start(yT[bass.ds(group, 1)].rearrange("a p s t n -> (a p) s t n"),
                                     y1[:, slot]).then_inc(y1_out[slot], 16)

            phases(sp, steps)
            sp.wait_ge(y1_done, STEPS)
            sp.dma_start(yT[GROUPS - 1], y1[:, 1]).then_inc(y1_out[1], 16)
            for slot in range(2):
                sp.wait_ge(y1_out[slot], 16 * GROUPS // 2)

        @block.gpsimd
        def _(pool):
            nc.gpsimd.memset(h_first[:, :, :], 0.0).then_inc(h_zeroed, 1)
            nc.gpsimd.memset(ifgc[:, 3], 0.0).then_inc(cell_zeroed, 1)
            for l in range(2):
                pool.wait_ge(largest_done, l + 1)
                nc.gpsimd.partition_all_reduce(largest_all[l][:, :], largest[l][:, :], P,
                                               bass.bass_isa.ReduceOp.max).then_inc(reduced, 1)

        @block.tensor
        def _(pe):
            def bulk0(bank, slot, b):
                for k in range(SUB):
                    last = nc.tensor.matmul(bulk0_ps[bank][:, 0:CHUNK * BATCH], wx0_sb[:, k, b, :], x_bulk[:, slot, k, :],
                                            start=(k == 0), stop=(k == SUB - 1))
                last.then_inc(bulk0_done, 1)

            pe.wait_ge(x_bulk_in[0], 16)
            for b in range(BLOCKS):
                if b >= 2:
                    pe.wait_ge(xw0_done, b - 1)
                for k in range(SUB):
                    if b == 0:
                        pe.wait_ge(wx0_in[k], 16)
                    last = nc.tensor.matmul(bulk0_ps[b % 2][:, 0:CHUNK * BATCH], wx0_sb[:, k, b, :], x_bulk[:, 0, k, :],
                                            start=(k == 0), stop=(k == SUB - 1))
                last.then_inc(bulk0_done, 1)

            def recurrent(out, width, states, weights):
                n = SUB * len(weights)
                i = 0
                for k in range(SUB):
                    for w in weights:
                        for q in range(QUADS):
                            last = nc.tensor.matmul(out[QUAD * q:QUAD * (q + 1), 0:width], states[:, k, :], w[:, k, q],
                                                    start=(i == 0), stop=(i == n - 1), tile_position=(0, QUAD * q))
                        i += 1
                return last

            def first(w_sb):
                return w_sb[:, :, :, :].rearrange("p k b (q c) -> p k q b c", q=QUADS)

            def steps(i, at, count):
                for j in range(count):
                    t, a = i * BODY + j, at + j
                    if a == 0:
                        pe.wait_ge(h_in, 16)
                        pe.wait_ge(wh0_in, 16)
                        recurrent(rec0_ps, BLOCKS * QUAD, h_first, [first(wh0_sb)]).then_inc(rec0_done, 1)
                    elif a < STEPS:
                        if a == 1:
                            pe.wait_ge(w_low, 2)
                        pe.wait_ge(h0_ready, t)
                        recurrent(rec0_ps, BLOCKS * QUAD, h0_parts, wh0_part).then_inc(rec0_done, 1)
                    v, c = divmod(a, CHUNK)
                    if v + 1 < CHUNKS:
                        if c == 0:
                            pe.wait_ge(x_bulk_in[(v + 1) % 2], loads(i, j, 1))
                        for m in range(BLOCKS_PER_STEP):
                            pe.wait_ge(xw0_done, t * BLOCKS_PER_STEP + (BLOCKS + m - 1))
                            bulk0((c * BLOCKS_PER_STEP + m) % 2, (v + 1) % 2, c * BLOCKS_PER_STEP + m)
                    if GROUP <= a < STEPS + GROUP:
                        g8, slot = a % GROUP, a // GROUP % 2 ^ 1
                        b, half = divmod(g8, GROUP // SUB)
                        if a == GROUP:
                            pe.wait_ge(wx1_in, 16)
                        if g8 == 0:
                            pe.wait_ge(y0_done, t)
                        if half == 0 and a >= GROUP + 4:
                            pe.wait_ge(xw1_done, t - (GROUP + 2))
                        for k in range(2 * half, 2 * half + 2):
                            last = nc.tensor.matmul(bulk1_ps[b % 2][:, 0:GROUP * BATCH], wx1_sb[:, k, b, :],
                                                    y0[:, slot, k].rearrange("p t n -> p (t n)"),
                                                    start=(k == 0), stop=(k == SUB - 1))
                        last.then_inc(bulk1_done, 1)
                    if a == LAG:
                        pe.wait_ge(wh1_in, 16)
                        recurrent(rec1_ps, SUB * QUAD, h_first, [first(wh1_sb)]).then_inc(rec1_done, 1)
                    elif a > LAG:
                        pe.wait_ge(h1_ready, t - LAG)
                        recurrent(rec1_ps, SUB * QUAD, h1_parts, wh1_part).then_inc(rec1_done, 1)

            phases(pe, steps)

        @block.vector
        def _(dve):
            dve.wait_ge(b_in, 32)
            nc.vector.tensor_scalar(b0_sb[:, 0:2 * SUB], b0_sb[:, 0:2 * SUB], 0.5, None, ALU.mult).then_inc(b0_halved, 1)
            nc.vector.tensor_scalar(b0_sb[:, 3 * SUB:], b0_sb[:, 3 * SUB:], 0.5, None, ALU.mult).then_inc(b0_halved, 1)
            for l, (w_sb, w_in) in enumerate(((wh0_sb, wh0_in), (wh1_sb, wh1_in))):
                dve.wait_ge(w_in, 16)
                nc.vector.tensor_reduce(largest[l][:, :], w_sb[:, :].rearrange("p k b c -> p (k b c)"),
                                        mybir.AxisListType.X, ALU.max, apply_absolute_value=True).then_inc(largest_done, 1)
            done = 0
            for l in range(2):
                dve.wait_ge(reduced, l + 1)
                nc.vector.tensor_scalar(largest_all[l][:, :], largest_all[l][:, :], 2.0 ** -100, None,
                                        ALU.max).then_inc(prep, 1)
                done += 1
                dve.wait_ge(prep, done)
                nc.vector.tensor_scalar(power[l][:, :].bitcast(i32), largest_all[l][:, :].bitcast(i32), 0x7F800000, None,
                                        ALU.bitwise_and).then_inc(prep, 1)
                done += 1
                dve.wait_ge(prep, done)
                nc.vector.tensor_scalar(w_scale[l][:, :].bitcast(i32), power[l][:, :].bitcast(i32), -1.0,
                                        float((2 * 127 + 14) << 23), ALU.mult, ALU.add).then_inc(prep, 1)
                nc.vector.tensor_scalar(unscale[l][:, :], power[l][:, :], 2.0 ** -14 / H_SCALE, None,
                                        ALU.mult).then_inc(prep, 1)
                done += 2
                dve.wait_ge(prep, done)
                if l == 0:
                    nc.vector.tensor_scalar(w_scale_half[:, :], w_scale[0][:, :], 0.5, None, ALU.mult).then_inc(prep, 1)
                    done += 1
                    dve.wait_ge(prep, done)
                nc.vector.tensor_copy(unscale[l][:, :], unscale[l][:, :]).then_inc(scaled, 1)
            for n, piece in enumerate(w_pieces()):
                dve.wait_ge(w_high, n + 1)
                w32, high, low, scale = w_piece(*piece)
                last = nc.vector.scalar_tensor_tensor(low, w32, scale, high, ALU.mult, ALU.subtract)
                if n == len(w_pieces()) - 1 or piece[0] != w_pieces()[n + 1][0]:
                    last.then_inc(w_low, 1)

            ifg = SUB * (GATES - 1)

            def lstm_step(t, a):
                c, slot = a % CHUNK, a // CHUNK % 2
                dve.wait_ge(rec0_done, t + 1)
                nc.vector.transpose(turned0[:, 0:ifg, :].rearrange("p b n -> p (b n)"),
                                    rec0_ps[:, 0:ifg * QUAD]).then_inc(turned_ifg, 1)
                nc.vector.transpose(turned0[:, ifg:, :].rearrange("p b n -> p (b n)"),
                                    rec0_ps[:, ifg * QUAD:]).then_inc(turned_o, 1)
                for sel, b_lo, b_hi, turned, summed, pre_done in (
                        ("ifg", 0, ifg, turned_ifg, sum_ifg, pre_ifg), ("o", ifg, BLOCKS, turned_o, sum_o, pre_o)):
                    cols = slice(b_lo * BATCH, b_hi * BATCH)
                    dve.wait_ge(turned, t + 1)
                    nc.vector.tensor_tensor(sum0[:, cols].rearrange("p (b n) -> p b n", n=BATCH),
                                            turned0[:, b_lo:b_hi, 0:BATCH], turned0[:, b_lo:b_hi, BATCH:],
                                            ALU.add).then_inc(summed, 1)
                    if c == 0 and sel == "ifg":
                        dve.wait_ge(xw0_done, t * BLOCKS_PER_STEP + BLOCKS)
                    dve.wait_ge(summed, t + 1)
                    if a == 0:
                        for lo, hi, s in (((0, 2 * SUB, 0.5), (2 * SUB, ifg, 1.0)) if sel == "ifg" else ((ifg, BLOCKS, 0.5),)):
                            part = slice(lo * BATCH, hi * BATCH)
                            last = nc.vector.scalar_tensor_tensor(pre0[:, part], sum0[:, part], s, xw0[:, 0, 0, part],
                                                                  ALU.mult, ALU.add)
                        last.then_inc(pre_done, 1)
                    else:
                        nc.vector.scalar_tensor_tensor(pre0[:, cols], sum0[:, cols], unscale[0][:, :], xw0[:, slot, c, cols],
                                                       ALU.mult, ALU.add).then_inc(pre_done, 1)
                dve.wait_ge(ifg_done, t + 1)
                if a == 0:
                    dve.wait_ge(cell_zeroed, 1)
                nc.vector.scalar_tensor_tensor(uv[:, :], ifgc[:, 0:2], 1.0, ifgc[:, 2:4], ALU.add, ALU.mult).then_inc(uv_done, 1)
                dve.wait_ge(uv_done, t + 1)
                nc.vector.scalar_tensor_tensor(ifgc[:, 3], uv[:, 1], 0.5, uv[:, 0], ALU.mult, ALU.add).then_inc(cell_done, 1)
                dve.wait_ge(o_done, t + 1)
                nc.vector.tensor_scalar(o_scaled[:, :], o_t[:, :], H_SCALE / 2, H_SCALE / 2, ALU.mult,
                                        ALU.add).then_inc(o_scaled_done, 1)
                dve.wait_ge(o_scaled_done, t + 1)
                dve.wait_ge(tanh_c_done, t + 1)
                nc.vector.tensor_tensor(h0_parts[:, :, 0:BATCH], o_scaled[:, :].rearrange("p (s n) -> p s n", n=BATCH),
                                        tanh_c[:, :].rearrange("p (s n) -> p s n", n=BATCH), ALU.mult).then_inc(h0_high, 1)
                nc.vector.tensor_tensor(h0_full[:, :], o_scaled[:, :], tanh_c[:, :], ALU.mult).then_inc(h0_full_done, 1)
                dve.wait_ge(h0_high, t + 1)
                dve.wait_ge(h0_full_done, t + 1)
                nc.vector.tensor_tensor(h0_parts[:, :, BATCH:], h0_full[:, :].rearrange("p (s n) -> p s n", n=BATCH),
                                        h0_parts[:, :, 0:BATCH], ALU.subtract).then_inc(h0_ready, 1)

            def rnn_step(n, a, stored):
                c, slot = a % GROUP, a // GROUP % 2
                dve.wait_ge(rec1_done, n)
                nc.vector.transpose(turned1[:, :, :].rearrange("p b n -> p (b n)"),
                                    rec1_ps[:, 0:SUB * QUAD]).then_inc(turned1_done, 1)
                dve.wait_ge(turned1_done, n)
                nc.vector.tensor_tensor(sum1[:, :].rearrange("p (b n) -> p b n", n=BATCH), turned1[:, :, 0:BATCH],
                                        turned1[:, :, BATCH:], ALU.add).then_inc(sum1_done, 1)
                dve.wait_ge(sum1_done, n)
                if c == 0:
                    dve.wait_ge(xw1_done, n + (GROUP - 1))
                nc.vector.scalar_tensor_tensor(pre1[:, :], sum1[:, :], 1.0 if a == 0 else unscale[1][:, :], xw1[:, slot, c],
                                               ALU.mult, ALU.add).then_inc(pre1_done, 1)
                dve.wait_ge(h1_full_done, n)
                full = h1_full[:, :].rearrange("p (s n) -> p s n", n=BATCH)
                nc.vector.tensor_scalar(h1_parts[:, :, 0:BATCH], full, H_SCALE, None, ALU.mult).then_inc(h1_high, 1)
                if c == 0 and a >= 2 * GROUP:
                    dve.wait_ge(y1_out[slot], stored)
                dve.wait_ge(h1_high, n)
                nc.vector.scalar_tensor_tensor(h1_parts[:, :, BATCH:], full, H_SCALE, h1_parts[:, :, 0:BATCH],
                                               ALU.mult, ALU.subtract).then_inc(h1_ready, 1)
                nc.vector.tensor_tensor(y1[:, slot, :, c], y0[:, slot, :, c], full, ALU.add).then_inc(y1_done, 1)

            def steps(i, at, count):
                for j in range(count):
                    t, a = i * BODY + j, at + j
                    if a < STEPS:
                        lstm_step(t, a)
                    if a >= LAG:
                        rnn_step(t - (LAG - 1), a - LAG, i * (16 * BODY // (2 * GROUP)) + 16 * ((j - LAG) // GROUP // 2))
                    if a < STEPS:
                        v = a // CHUNK
                        if a % CHUNK == 0:
                            dve.wait_ge(x_res_in[v % 2], loads(i, j, 0))
                        if a % GROUP == 0 and a >= LAG:
                            dve.wait_ge(bulk1_done, t - GROUP)
                        if a >= LAG:
                            dve.wait_ge(y1_done, t - (LAG - 1))
                        nc.vector.scalar_tensor_tensor(y0[:, a // GROUP % 2, :, a % GROUP],
                                                       h0_full[:, :].rearrange("p (s n) -> p s n", n=BATCH), 1.0 / H_SCALE,
                                                       x_res[:, v % 2, :, a % CHUNK], ALU.mult, ALU.add).then_inc(y0_done, 1)

            phases(dve, steps)

        @block.scalar
        def _(act):
            def evacuate0(bank, slot, b):
                out = xw0[:, slot, :, b * BATCH:(b + 1) * BATCH]
                nc.scalar.activation(out, bulk0_ps[bank][:, 0:CHUNK * BATCH].rearrange("p (t n) -> p t n", n=BATCH),
                                     ACT.Identity, bias=b0_sb[:, b:b + 1],
                                     scale=1.0 if b // SUB == 2 else 0.5).then_inc(xw0_done, 1)

            act.wait_ge(b0_halved, 2)
            high_at = 0
            for b in range(BLOCKS):
                act.wait_ge(bulk0_done, b + 1)
                evacuate0(b % 2, 0, b)
            act.wait_ge(scaled, 1)
            for piece in w_pieces():
                if piece[:3] == (1, 0, 0):
                    act.wait_ge(scaled, 2)
                w32, high, low, scale = w_piece(*piece)
                nc.scalar.activation(high, w32, ACT.Copy, scale=scale).then_inc(w_high, 1)

            def steps(i, at, count):
                for j in range(count):
                    t, a = i * BODY + j, at + j
                    if a < STEPS:
                        act.wait_ge(pre_ifg, t + 1)
                        nc.scalar.activation(ifgc[:, 0:3].rearrange("p g n -> p (g n)"), pre0[:, 0:SIG],
                                             ACT.Tanh).then_inc(ifg_done, 1)
                        act.wait_ge(pre_o, t + 1)
                        nc.scalar.activation(o_t[:, :], pre0[:, SIG:], ACT.Tanh).then_inc(o_done, 1)
                        act.wait_ge(cell_done, t + 1)
                        nc.scalar.activation(tanh_c[:, :], ifgc[:, 3], ACT.Tanh, scale=0.5).then_inc(tanh_c_done, 1)
                    v, c = divmod(a, CHUNK)
                    if v + 1 < CHUNKS:
                        for m in range(BLOCKS_PER_STEP):
                            b = c * BLOCKS_PER_STEP + m
                            act.wait_ge(bulk0_done, t * BLOCKS_PER_STEP + (BLOCKS + m + 1))
                            evacuate0(b % 2, (v + 1) % 2, b)
                    if GROUP <= a < STEPS + GROUP and a % 2:
                        b, slot = a % GROUP // 2, a // GROUP % 2 ^ 1
                        act.wait_ge(bulk1_done, t - (GROUP - 1))
                        nc.scalar.activation(xw1[:, slot, :, b * BATCH:(b + 1) * BATCH],
                                             bulk1_ps[b % 2][:, 0:GROUP * BATCH].rearrange("p (t n) -> p t n", n=BATCH),
                                             ACT.Identity, bias=b1_sb[:, b:b + 1], scale=1.0).then_inc(xw1_done, 2)
                    if a >= LAG:
                        act.wait_ge(pre1_done, t - (LAG - 1))
                        nc.scalar.activation(h1_full[:, :], pre1[:, :], ACT.Tanh).then_inc(h1_full_done, 1)

            phases(act, steps)


def kernel(x, cond_1024, L0_cond_Wx, L0_cond_Wh, L0_cond_b, L1_cond_Wx, L1_cond_Wh, L1_cond_b):
    import concourse.bacc as bacc
    from concourse.bass_utils import run_bass_kernel_spmd

    def laid(a, shape, order):
        return np.ascontiguousarray(np.asarray(a).reshape(shape).transpose(order))

    def gates(a):
        a = np.asarray(a)
        return a.reshape(*a.shape[:-1], GATES, DIM)[..., GATE_ORDER, :].reshape(a.shape)

    arrays = {
        "xT": laid(x, (BATCH, CHUNKS, CHUNK, SUB, P), (1, 4, 3, 2, 0)),
        "h0T": laid(cond_1024, (BATCH, SUB, P), (2, 1, 0)),
        "wx0": laid(gates(L0_cond_Wx), (SUB, P, BLOCKS, P), (1, 0, 2, 3)),
        "wh0": laid(gates(L0_cond_Wh), (SUB, P, BLOCKS, P), (1, 0, 2, 3)),
        "b0": laid(gates(L0_cond_b), (BLOCKS, P), (1, 0)),
        "wx1": laid(L1_cond_Wx, (SUB, P, SUB, P), (1, 0, 2, 3)),
        "wh1": laid(L1_cond_Wh, (SUB, P, SUB, P), (1, 0, 2, 3)),
        "b1": laid(L1_cond_b, (SUB, P), (1, 0)),
    }
    nc = bacc.Bacc("TRN2", target_bir_lowering=False, num_devices=1)
    args = [nc.dram_tensor(n, a.shape, mybir.dt.from_np(a.dtype), kind="ExternalInput").ap() for n, a in arrays.items()]
    out = nc.dram_tensor("yT", (GROUPS, P, SUB, GROUP, BATCH), fp32, kind="ExternalOutput").ap()
    residual_lstm_rnn(nc, *args, out)
    r = run_bass_kernel_spmd(nc, [arrays], core_ids=[0])
    y = np.asarray(r.results[0]["yT"])
    return np.ascontiguousarray(y.transpose(4, 0, 3, 2, 1)).reshape(BATCH, STEPS, DIM)
```

```python
from contextlib import ExitStack

import numpy as np

import concourse.bass as bass
from concourse import mybir

BATCH, STEPS, DIM = 16, 512, 512
P = 128
SUB = DIM // P
QUADS, QUAD = 4, 32
GATES = 4
HALVES = 2
SUBH = SUB // HALVES
BLOCKS = GATES * SUB
BLOCKSH = BLOCKS // HALVES
CHUNK = 16
GROUP = 8
LAG = 2 * GROUP
BODY = 2 * CHUNK
CHUNKS = STEPS // CHUNK
GROUPS = STEPS // GROUP
BLOCKS_PER_STEP = BLOCKS // CHUNK
H_SCALE = 2.0 ** 15
CELL = SUB * BATCH
CELLH = CELL // HALVES

fp32, fp16, i32 = mybir.dt.float32, mybir.dt.float16, mybir.dt.int32
ALU = mybir.AluOpType
ACT = mybir.ActivationFunctionType


def residual_lstm_rnn(nc, xT, h0T, wx0, wh0, b0, wx1, wh1, b1, yT):
    with ExitStack() as ctx:
        def sb(name, shape, dt=fp32):
            return ctx.enter_context(nc.sbuf_tensor(name, shape, dt))

        def pb(name):
            return ctx.enter_context(nc.psum_tensor(name, [P, 512], fp32))

        def sem(name):
            return ctx.enter_context(nc.semaphore(name))

        wx0_sb = sb("wx0_sb", [P, SUB, BLOCKS, P])
        wh0_sb = sb("wh0_sb", [P, SUB, BLOCKS, P])
        wx1_sb = sb("wx1_sb", [P, SUB, SUB, P])
        wh1_sb = sb("wh1_sb", [P, SUB, SUB, P])
        wh0_part = [sb(f"wh0_part{i}", [P, SUB, QUADS, BLOCKS * QUAD], fp16) for i in range(2)]
        wh1_part = [sb(f"wh1_part{i}", [P, SUB, SUB * P], fp16) for i in range(2)]
        b0_sb = sb("b0_sb", [P, BLOCKS])
        b1_sb = sb("b1_sb", [P, SUB])
        largest = [sb(f"largest{l}", [P, 1]) for l in range(2)]
        largest_all = [sb(f"largest_all{l}", [P, 1]) for l in range(2)]
        power = [sb(f"power{l}", [P, 1]) for l in range(2)]
        w_scale = [sb(f"w_scale{l}", [P, 1]) for l in range(2)]
        w_scale_half = sb("w_scale_half", [P, 1])
        unscale = [sb(f"unscale{l}", [P, 1]) for l in range(2)]
        h_first = sb("h_first", [P, SUB, 2 * BATCH])
        h0_parts = sb("h0_parts", [P, SUB, 2 * BATCH], fp16)
        h1_parts = sb("h1_parts", [P, SUB, 2 * BATCH], fp16)
        x_bulk = sb("x_bulk", [P, 2, SUB, CHUNK * BATCH])
        x_res = sb("x_res", [P, 2, SUB, CHUNK, BATCH])
        xw0 = sb("xw0", [P, 2, CHUNK, BLOCKS * BATCH])
        y0 = sb("y0", [P, 2, SUB, GROUP, BATCH])
        xw1 = sb("xw1", [P, 2, GROUP, CELL])
        y1 = sb("y1", [P, 2, SUB, GROUP, BATCH])
        turned0 = sb("turned0", [P, BLOCKS, 2 * BATCH])
        sum0 = sb("sum0", [P, HALVES, BLOCKSH * BATCH])
        pre0 = sb("pre0", [P, HALVES, BLOCKSH * BATCH])
        gates_cell = sb("gates_cell", [P, HALVES, GATES + 1, CELLH])
        uv = sb("uv", [P, HALVES, 2, CELLH])
        o_scaled = sb("o_scaled", [P, HALVES, CELLH])
        tanh_c = sb("tanh_c", [P, HALVES, CELLH])
        h0_full = sb("h0_full", [P, CELL])
        sum1 = sb("sum1", [P, CELL])
        pre1 = sb("pre1", [P, CELL])
        h1_full = sb("h1_full", [P, CELL])

        rec0_ps, rec1_ps = pb("rec0_ps"), pb("rec1_ps")
        bulk0_ps = [pb(f"bulk0_ps{i}") for i in range(2)]
        bulk1_ps = [pb(f"bulk1_ps{i}") for i in range(2)]

        wx0_in = [sem(f"wx0_in{k}") for k in range(SUB)]
        wh0_in, wh1_in, wx1_in, b_in, h_in = (sem(n) for n in ("wh0_in", "wh1_in", "wx1_in", "b_in", "h_in"))
        h_zeroed, cell_zeroed, b0_halved = sem("h_zeroed"), sem("cell_zeroed"), sem("b0_halved")
        prep, largest_done, reduced = sem("prep"), sem("largest_done"), sem("reduced")
        scaled, w_high, w_low = sem("scaled"), sem("w_high"), sem("w_low")
        x_bulk_in = [sem(f"x_bulk_in{i}") for i in range(2)]
        x_res_in = [sem(f"x_res_in{i}") for i in range(2)]
        y1_out = [sem(f"y1_out{i}") for i in range(2)]
        def sem_by_half(name):
            return [sem(f"{name}_{half}") for half in range(HALVES)]

        rec0_done = sem("rec0_done")
        turned0_done, sum0_done, pre0_done = (sem_by_half(n) for n in ("turned0_done", "sum0_done", "pre0_done"))
        gates_done, uv_done, cell_done = (sem_by_half(n) for n in ("gates_done", "uv_done", "cell_done"))
        o_scaled_done, tanh_c_done = sem_by_half("o_scaled_done"), sem_by_half("tanh_c_done")
        h0_full_done, h0_ready = sem_by_half("h0_full_done"), sem_by_half("h0_ready")
        y0_done = sem("y0_done")
        bulk0_done, xw0_done = sem("bulk0_done"), sem("xw0_done")
        bulk1_done, xw1_done = sem("bulk1_done"), sem("xw1_done")
        rec1_done, sum1_done, pre1_done = sem("rec1_done"), sem("sum1_done"), sem("pre1_done")
        h1_full_done, h1_high, h1_ready, y1_done = (
            sem("h1_full_done"), sem("h1_high"), sem("h1_ready"), sem("y1_done"))

        def phases(eng, steps):
            steps(0, 0, BODY)
            with eng.Fori(1, STEPS // BODY - 1) as i:
                steps(i, BODY, BODY)
            steps(STEPS // BODY - 1, STEPS - BODY, BODY)
            steps(STEPS // BODY, STEPS, LAG)

        def loads(i, j, ahead):
            return i * 16 + 16 * ((j // CHUNK + ahead) // 2 + 1)

        def is_g(b):
            return b % BLOCKSH // SUBH == GATES - 1

        def w_pieces():
            return ([(0, k, q, lo, hi) for k in range(SUB) for q in range(QUADS) for half in range(0, BLOCKS, BLOCKSH)
                     for lo, hi in ((half, half + BLOCKSH - SUBH), (half + BLOCKSH - SUBH, half + BLOCKSH))]
                    + [(1, k, 0, 0, SUB) for k in range(SUB)])

        def w_piece(l, k, q, lo, hi):
            if l == 1:
                return wh1_sb[:, k].rearrange("p b c -> p (b c)"), wh1_part[0][:, k], wh1_part[1][:, k], w_scale[1][:, :]
            w32 = wh0_sb[:, k, lo:hi, QUAD * q:QUAD * (q + 1)]
            high, low = (h[:, k, q].rearrange("p (b c) -> p b c", c=QUAD)[:, lo:hi] for h in wh0_part)
            return w32, high, low, (w_scale[0] if is_g(lo) else w_scale_half)[:, :]


        block = ctx.enter_context(nc.Block())

        @block.sync
        def _(sp):
            for k in range(SUB):
                sp.dma_start(wx0_sb[:, k], wx0[:, k]).then_inc(wx0_in[k], 16)
                if k == 0:
                    sp.dma_start(x_bulk[:, 0], xT[0].rearrange("p s t n -> p s (t n)")).then_inc(x_bulk_in[0], 16)
                    sp.dma_start(b0_sb[:, :], b0).then_inc(b_in, 16)
                    sp.dma_start(b1_sb[:, :], b1).then_inc(b_in, 16)
            sp.dma_start(wh0_sb[:, :], wh0).then_inc(wh0_in, 16)
            sp.dma_start(wh1_sb[:, :], wh1).then_inc(wh1_in, 16)
            sp.wait_ge(h_zeroed, 1)
            sp.dma_start(h_first[:, :, 0:BATCH], h0T).then_inc(h_in, 16)
            sp.dma_start(x_res[:, 0], xT[0]).then_inc(x_res_in[0], 16)
            sp.dma_start(x_bulk[:, 1], xT[1].rearrange("p s t n -> p s (t n)")).then_inc(x_bulk_in[1], 16)
            sp.dma_start(wx1_sb[:, :], wx1).then_inc(wx1_in, 16)

            def steps(i, at, count):
                for j in range(0, count, GROUP):
                    t, a = i * BODY + j, at + j
                    v = a // CHUNK
                    if a % CHUNK == 0 and v + 1 < CHUNKS:
                        if a:
                            sp.wait_ge(y0_done, t)
                        chunk = i * (BODY // CHUNK) + j // CHUNK
                        sp.dma_start(x_res[:, (v + 1) % 2], xT[bass.ds(chunk + 1, 1)].rearrange("a p s t n -> (a p) s t n")
                                     ).then_inc(x_res_in[(v + 1) % 2], 16)
                        if v + 2 < CHUNKS:
                            sp.wait_ge(bulk0_done, t * BLOCKS_PER_STEP + BLOCKS)
                            sp.dma_start(x_bulk[:, v % 2], xT[bass.ds(chunk + 2, 1)].rearrange("a p s t n -> (a p) s (t n)")
                                         ).then_inc(x_bulk_in[v % 2], 16)
                    if a >= LAG + GROUP:
                        slot = a // GROUP % 2 ^ 1
                        sp.wait_ge(y1_done, t - LAG)
                        group = i * (BODY // GROUP) + ((j - LAG) // GROUP - 1)
                        sp.dma_start(yT[bass.ds(group, 1)].rearrange("a p s t n -> (a p) s t n"),
                                     y1[:, slot]).then_inc(y1_out[slot], 16)

            phases(sp, steps)
            sp.wait_ge(y1_done, STEPS)
            sp.dma_start(yT[GROUPS - 1], y1[:, 1]).then_inc(y1_out[1], 16)
            for slot in range(2):
                sp.wait_ge(y1_out[slot], 16 * GROUPS // 2)

        @block.gpsimd
        def _(pool):
            nc.gpsimd.memset(h_first[:, :, :], 0.0).then_inc(h_zeroed, 1)
            nc.gpsimd.memset(gates_cell[:, :, GATES], 0.0).then_inc(cell_zeroed, 1)
            for l in range(2):
                pool.wait_ge(largest_done, l + 1)
                nc.gpsimd.partition_all_reduce(largest_all[l][:, :], largest[l][:, :], P,
                                               bass.bass_isa.ReduceOp.max).then_inc(reduced, 1)

        @block.tensor
        def _(pe):
            def bulk0(bank, slot, b):
                for k in range(SUB):
                    last = nc.tensor.matmul(bulk0_ps[bank][:, 0:CHUNK * BATCH], wx0_sb[:, k, b, :], x_bulk[:, slot, k, :],
                                            start=(k == 0), stop=(k == SUB - 1))
                last.then_inc(bulk0_done, 1)

            pe.wait_ge(x_bulk_in[0], 16)
            for b in range(BLOCKS):
                if b >= 2:
                    pe.wait_ge(xw0_done, b - 1)
                for k in range(SUB):
                    if b == 0:
                        pe.wait_ge(wx0_in[k], 16)
                    last = nc.tensor.matmul(bulk0_ps[b % 2][:, 0:CHUNK * BATCH], wx0_sb[:, k, b, :], x_bulk[:, 0, k, :],
                                            start=(k == 0), stop=(k == SUB - 1))
                last.then_inc(bulk0_done, 1)

            def recurrent0(states, weights, ready):
                passes = SUB * len(weights)
                for n in range(passes):
                    k, w = divmod(n, len(weights))
                    if w == 0 and k % SUBH == 0:
                        ready(k // SUBH)
                    for q in range(QUADS):
                        last = nc.tensor.matmul(rec0_ps[QUAD * q:QUAD * (q + 1), :], states[:, k, :], weights[w][:, k, q],
                                                start=(n == 0), stop=(n == passes - 1), tile_position=(0, QUAD * q))
                last.then_inc(rec0_done, 1)

            def recurrent1(states, weights):
                passes = SUB * len(weights)
                for b in range(SUB):
                    for n in range(passes):
                        k, w = divmod(n, len(weights))
                        last = nc.tensor.matmul(rec1_ps[:, b * 2 * BATCH:(b + 1) * 2 * BATCH], weights[w][:, k, b * P:(b + 1) * P],
                                                states[:, k, :], start=(n == 0), stop=(n == passes - 1))
                last.then_inc(rec1_done, 1)

            def steps(i, at, count):
                for j in range(count):
                    t, a = i * BODY + j, at + j
                    if a == 0:
                        pe.wait_ge(h_in, 16)
                        pe.wait_ge(wh0_in, 16)
                        recurrent0(h_first, [wh0_sb[:, :, :, :].rearrange("p k b (q c) -> p k q b c", q=QUADS)],
                                   lambda half: None)
                    elif a < STEPS:
                        if a == 1:
                            pe.wait_ge(w_low, 2)
                        recurrent0(h0_parts, wh0_part, lambda half: pe.wait_ge(h0_ready[half], t))
                    v, c = divmod(a, CHUNK)
                    if v + 1 < CHUNKS:
                        if c == 0:
                            pe.wait_ge(x_bulk_in[(v + 1) % 2], loads(i, j, 1))
                        for m in range(BLOCKS_PER_STEP):
                            pe.wait_ge(xw0_done, t * BLOCKS_PER_STEP + (BLOCKS + m - 1))
                            bulk0((c * BLOCKS_PER_STEP + m) % 2, (v + 1) % 2, c * BLOCKS_PER_STEP + m)
                    if GROUP <= a < STEPS + GROUP:
                        g8, slot = a % GROUP, a // GROUP % 2 ^ 1
                        b, half = divmod(g8, GROUP // SUB)
                        if a == GROUP:
                            pe.wait_ge(wx1_in, 16)
                        if g8 == 0:
                            pe.wait_ge(y0_done, t)
                        if half == 0 and a >= GROUP + 4:
                            pe.wait_ge(xw1_done, t - (GROUP + 2))
                        for k in range(2 * half, 2 * half + 2):
                            last = nc.tensor.matmul(bulk1_ps[b % 2][:, 0:GROUP * BATCH], wx1_sb[:, k, b, :],
                                                    y0[:, slot, k].rearrange("p t n -> p (t n)"),
                                                    start=(k == 0), stop=(k == SUB - 1))
                        last.then_inc(bulk1_done, 1)
                    if a == LAG:
                        pe.wait_ge(wh1_in, 16)
                        recurrent1(h_first, [wh1_sb[:, :].rearrange("p k b c -> p k (b c)")])
                    elif a > LAG:
                        pe.wait_ge(h1_ready, t - LAG)
                        recurrent1(h1_parts, wh1_part)

            phases(pe, steps)

        @block.vector
        def _(dve):
            dve.wait_ge(b_in, 32)
            halved = b0_sb[:, :].rearrange("p (h b) -> p h b", h=HALVES)[:, :, 0:BLOCKSH - SUBH]
            nc.vector.tensor_scalar(halved, halved, 0.5, None, ALU.mult).then_inc(b0_halved, 1)
            for l, (w_sb, w_in) in enumerate(((wh0_sb, wh0_in), (wh1_sb, wh1_in))):
                dve.wait_ge(w_in, 16)
                nc.vector.tensor_reduce(largest[l][:, :], w_sb[:, :].rearrange("p k b c -> p (k b c)"),
                                        mybir.AxisListType.X, ALU.max, apply_absolute_value=True).then_inc(largest_done, 1)
            done = 0
            for l in range(2):
                dve.wait_ge(reduced, l + 1)
                nc.vector.tensor_scalar(largest_all[l][:, :], largest_all[l][:, :], 2.0 ** -100, None,
                                        ALU.max).then_inc(prep, 1)
                done += 1
                dve.wait_ge(prep, done)
                nc.vector.tensor_scalar(power[l][:, :].bitcast(i32), largest_all[l][:, :].bitcast(i32), 0x7F800000, None,
                                        ALU.bitwise_and).then_inc(prep, 1)
                done += 1
                dve.wait_ge(prep, done)
                nc.vector.tensor_scalar(w_scale[l][:, :].bitcast(i32), power[l][:, :].bitcast(i32), -1.0,
                                        float((2 * 127 + 14) << 23), ALU.mult, ALU.add).then_inc(prep, 1)
                nc.vector.tensor_scalar(unscale[l][:, :], power[l][:, :], 2.0 ** -14 / H_SCALE, None,
                                        ALU.mult).then_inc(prep, 1)
                done += 2
                dve.wait_ge(prep, done)
                if l == 0:
                    nc.vector.tensor_scalar(w_scale_half[:, :], w_scale[0][:, :], 0.5, None, ALU.mult).then_inc(prep, 1)
                    done += 1
                    dve.wait_ge(prep, done)
                nc.vector.tensor_copy(unscale[l][:, :], unscale[l][:, :]).then_inc(scaled, 1)
            for n, piece in enumerate(w_pieces()):
                dve.wait_ge(w_high, n + 1)
                w32, high, low, scale = w_piece(*piece)
                last = nc.vector.scalar_tensor_tensor(low, w32, scale, high, ALU.mult, ALU.subtract)
                if n == len(w_pieces()) - 1 or piece[0] != w_pieces()[n + 1][0]:
                    last.then_inc(w_low, 1)

            def slices(ap):
                return ap.rearrange("p (s n) -> p s n", n=BATCH)

            def turn0(half, part, parts):
                lo = half * BLOCKSH + part * BLOCKSH // parts
                hi = lo + BLOCKSH // parts
                return nc.vector.transpose(turned0[:, lo:hi].rearrange("p b n -> p (b n)"), rec0_ps[:, lo * QUAD:hi * QUAD])

            def add_parts0(half, n):
                dve.wait_ge(turned0_done[half], n)
                blocks = turned0[:, half * BLOCKSH:(half + 1) * BLOCKSH]
                nc.vector.tensor_tensor(slices(sum0[:, half]), blocks[:, :, 0:BATCH], blocks[:, :, BATCH:],
                                        ALU.add).then_inc(sum0_done[half], 1)

            def add_xw0(half, n, a):
                dve.wait_ge(sum0_done[half], n)
                cols = slice(half * BLOCKSH * BATCH, (half + 1) * BLOCKSH * BATCH)
                xw = xw0[:, a // CHUNK % 2, a % CHUNK, cols]
                if a:
                    nc.vector.scalar_tensor_tensor(pre0[:, half], sum0[:, half], unscale[0][:, :], xw,
                                                   ALU.mult, ALU.add).then_inc(pre0_done[half], 1)
                else:
                    sig = (GATES - 1) * CELLH
                    nc.vector.scalar_tensor_tensor(pre0[:, half, 0:sig], sum0[:, half, 0:sig], 0.5, xw[:, 0:sig],
                                                   ALU.mult, ALU.add)
                    nc.vector.tensor_tensor(pre0[:, half, sig:], sum0[:, half, sig:], xw[:, sig:],
                                            ALU.add).then_inc(pre0_done[half], 1)

            def gate_products(half, n):
                dve.wait_ge(gates_done[half], n)
                nc.vector.scalar_tensor_tensor(uv[:, half], gates_cell[:, half, 0:2], 1.0, gates_cell[:, half, 3:5],
                                               ALU.add, ALU.mult).then_inc(uv_done[half], 1)
                nc.vector.tensor_scalar(o_scaled[:, half], gates_cell[:, half, 2], H_SCALE / 2, H_SCALE / 2, ALU.mult,
                                        ALU.add).then_inc(o_scaled_done[half], 1)

            def cell(half, n):
                dve.wait_ge(uv_done[half], n)
                nc.vector.scalar_tensor_tensor(gates_cell[:, half, GATES], uv[:, half, 1], 0.5, uv[:, half, 0],
                                               ALU.mult, ALU.add).then_inc(cell_done[half], 1)

            def state_cols(half):
                return slice(half * CELLH, (half + 1) * CELLH), slice(half * SUBH, (half + 1) * SUBH)

            def state_high(half, n):
                cols, subs = state_cols(half)
                dve.wait_ge(o_scaled_done[half], n)
                dve.wait_ge(tanh_c_done[half], n)
                nc.vector.tensor_tensor(h0_parts[:, subs, 0:BATCH], slices(o_scaled[:, half]), slices(tanh_c[:, half]), ALU.mult)
                nc.vector.tensor_tensor(h0_full[:, cols], o_scaled[:, half], tanh_c[:, half],
                                        ALU.mult).then_inc(h0_full_done[half], 1)

            def state_low(half, n):
                cols, subs = state_cols(half)
                dve.wait_ge(h0_full_done[half], n)
                nc.vector.tensor_tensor(h0_parts[:, subs, BATCH:], slices(h0_full[:, cols]), h0_parts[:, subs, 0:BATCH],
                                        ALU.subtract).then_inc(h0_ready[half], 1)

            def lstm_step(t, a):
                n = t + 1
                if a % CHUNK == 0:
                    dve.wait_ge(xw0_done, t * BLOCKS_PER_STEP + BLOCKS)
                dve.wait_ge(rec0_done, n)
                turn0(0, 0, 1).then_inc(turned0_done[0], 1)
                turn0(1, 0, 2)
                add_parts0(0, n)
                turn0(1, 1, 2).then_inc(turned0_done[1], 1)
                add_xw0(0, n, a)
                add_parts0(1, n)
                add_xw0(1, n, a)
                if a == 0:
                    dve.wait_ge(cell_zeroed, 1)
                gate_products(0, n)
                cell(0, n)
                gate_products(1, n)
                cell(1, n)
                state_high(0, n)
                state_low(0, n)
                state_high(1, n)
                state_low(1, n)

            def rnn_step(n, a, stored):
                c, slot = a % GROUP, a // GROUP % 2
                dve.wait_ge(rec1_done, n)
                product = rec1_ps[:, 0:SUB * 2 * BATCH].rearrange("p (b n) -> p b n", n=2 * BATCH)
                if c == 0:
                    dve.wait_ge(xw1_done, n + (GROUP - 1))
                scale = 1.0 if a == 0 else unscale[1][:, :]
                nc.vector.scalar_tensor_tensor(slices(sum1[:, :]), product[:, :, BATCH:], scale, slices(xw1[:, slot, c]),
                                               ALU.mult, ALU.add).then_inc(sum1_done, 1)
                dve.wait_ge(sum1_done, n)
                nc.vector.scalar_tensor_tensor(slices(pre1[:, :]), product[:, :, 0:BATCH], scale, slices(sum1[:, :]),
                                               ALU.mult, ALU.add).then_inc(pre1_done, 1)
                dve.wait_ge(h1_full_done, n)
                full = h1_full[:, :].rearrange("p (s n) -> p s n", n=BATCH)
                nc.vector.tensor_scalar(h1_parts[:, :, 0:BATCH], full, H_SCALE, None, ALU.mult).then_inc(h1_high, 1)
                if c == 0 and a >= 2 * GROUP:
                    dve.wait_ge(y1_out[slot], stored)
                dve.wait_ge(h1_high, n)
                nc.vector.scalar_tensor_tensor(h1_parts[:, :, BATCH:], full, H_SCALE, h1_parts[:, :, 0:BATCH],
                                               ALU.mult, ALU.subtract).then_inc(h1_ready, 1)
                nc.vector.tensor_tensor(y1[:, slot, :, c], y0[:, slot, :, c], full, ALU.add).then_inc(y1_done, 1)

            def steps(i, at, count):
                for j in range(count):
                    t, a = i * BODY + j, at + j
                    if a < STEPS:
                        lstm_step(t, a)
                    if a >= LAG:
                        rnn_step(t - (LAG - 1), a - LAG, i * (16 * BODY // (2 * GROUP)) + 16 * ((j - LAG) // GROUP // 2))
                    if a < STEPS:
                        v = a // CHUNK
                        if a % CHUNK == 0:
                            dve.wait_ge(x_res_in[v % 2], loads(i, j, 0))
                        if a % GROUP == 0 and a >= LAG:
                            dve.wait_ge(bulk1_done, t - GROUP)
                        if a >= LAG:
                            dve.wait_ge(y1_done, t - (LAG - 1))
                        nc.vector.scalar_tensor_tensor(y0[:, a // GROUP % 2, :, a % GROUP],
                                                       h0_full[:, :].rearrange("p (s n) -> p s n", n=BATCH), 1.0 / H_SCALE,
                                                       x_res[:, v % 2, :, a % CHUNK], ALU.mult, ALU.add).then_inc(y0_done, 1)

            phases(dve, steps)

        @block.scalar
        def _(act):
            def evacuate0(bank, slot, b):
                out = xw0[:, slot, :, b * BATCH:(b + 1) * BATCH]
                nc.scalar.activation(out, bulk0_ps[bank][:, 0:CHUNK * BATCH].rearrange("p (t n) -> p t n", n=BATCH),
                                     ACT.Identity, bias=b0_sb[:, b:b + 1],
                                     scale=1.0 if is_g(b) else 0.5).then_inc(xw0_done, 1)

            act.wait_ge(b0_halved, 1)
            pieces, per_block = w_pieces(), len(w_pieces()) // (BLOCKS - BLOCKS // 2)
            for b in range(BLOCKS):
                act.wait_ge(bulk0_done, b + 1)
                evacuate0(b % 2, 0, b)
                if b < BLOCKS // 2:
                    continue
                for piece in pieces[:per_block] if b < BLOCKS - 1 else pieces:
                    act.wait_ge(scaled, piece[0] + 1)
                    w32, high, low, scale = w_piece(*piece)
                    nc.scalar.activation(high, w32, ACT.Copy, scale=scale).then_inc(w_high, 1)
                del pieces[:per_block]

            def steps(i, at, count):
                for j in range(count):
                    t, a = i * BODY + j, at + j
                    if a < STEPS:
                        for half in range(HALVES):
                            act.wait_ge(pre0_done[half], t + 1)
                            nc.scalar.activation(gates_cell[:, half, 0:GATES].rearrange("p g n -> p (g n)"), pre0[:, half],
                                                 ACT.Tanh).then_inc(gates_done[half], 1)
                        for half in range(HALVES):
                            act.wait_ge(cell_done[half], t + 1)
                            nc.scalar.activation(tanh_c[:, half], gates_cell[:, half, GATES], ACT.Tanh,
                                                 scale=0.5).then_inc(tanh_c_done[half], 1)
                    v, c = divmod(a, CHUNK)
                    if v + 1 < CHUNKS:
                        for m in range(BLOCKS_PER_STEP):
                            b = c * BLOCKS_PER_STEP + m
                            act.wait_ge(bulk0_done, t * BLOCKS_PER_STEP + (BLOCKS + m + 1))
                            evacuate0(b % 2, (v + 1) % 2, b)
                    if GROUP <= a < STEPS + GROUP and a % 2:
                        b, slot = a % GROUP // 2, a // GROUP % 2 ^ 1
                        act.wait_ge(bulk1_done, t - (GROUP - 1))
                        nc.scalar.activation(xw1[:, slot, :, b * BATCH:(b + 1) * BATCH],
                                             bulk1_ps[b % 2][:, 0:GROUP * BATCH].rearrange("p (t n) -> p t n", n=BATCH),
                                             ACT.Identity, bias=b1_sb[:, b:b + 1], scale=1.0).then_inc(xw1_done, 2)
                    if a >= LAG:
                        act.wait_ge(pre1_done, t - (LAG - 1))
                        nc.scalar.activation(h1_full[:, :], pre1[:, :], ACT.Tanh).then_inc(h1_full_done, 1)

            phases(act, steps)


def kernel(x, cond_1024, L0_cond_Wx, L0_cond_Wh, L0_cond_b, L1_cond_Wx, L1_cond_Wh, L1_cond_b):
    import concourse.bacc as bacc
    from concourse.bass_utils import run_bass_kernel_spmd

    def laid(a, shape, order):
        return np.ascontiguousarray(np.asarray(a).reshape(shape).transpose(order))

    def gates(a):
        a = np.asarray(a)
        return a.reshape(*a.shape[:-1], GATES, HALVES, SUBH * P).swapaxes(-3, -2).reshape(a.shape)

    arrays = {
        "xT": laid(x, (BATCH, CHUNKS, CHUNK, SUB, P), (1, 4, 3, 2, 0)),
        "h0T": laid(cond_1024, (BATCH, SUB, P), (2, 1, 0)),
        "wx0": laid(gates(L0_cond_Wx), (SUB, P, BLOCKS, P), (1, 0, 2, 3)),
        "wh0": laid(gates(L0_cond_Wh), (SUB, P, BLOCKS, P), (1, 0, 2, 3)),
        "b0": laid(gates(L0_cond_b), (BLOCKS, P), (1, 0)),
        "wx1": laid(L1_cond_Wx, (SUB, P, SUB, P), (1, 0, 2, 3)),
        "wh1": laid(L1_cond_Wh, (SUB, P, SUB, P), (1, 0, 2, 3)),
        "b1": laid(L1_cond_b, (SUB, P), (1, 0)),
    }
    nc = bacc.Bacc("TRN2", target_bir_lowering=False, num_devices=1)
    args = [nc.dram_tensor(n, a.shape, mybir.dt.from_np(a.dtype), kind="ExternalInput").ap() for n, a in arrays.items()]
    out = nc.dram_tensor("yT", (GROUPS, P, SUB, GROUP, BATCH), fp32, kind="ExternalOutput").ap()
    residual_lstm_rnn(nc, *args, out)
    r = run_bass_kernel_spmd(nc, [arrays], core_ids=[0])
    y = np.asarray(r.results[0]["yT"])
    return np.ascontiguousarray(y.transpose(4, 0, 3, 2, 1)).reshape(BATCH, STEPS, DIM)
```

```python
from contextlib import ExitStack

import numpy as np

import concourse.bass as bass
from concourse import mybir

BATCH, STEPS, DIM = 16, 512, 512
P = 128
SUB = DIM // P
QUADS, QUAD = 4, 32
GATES = 4
HALVES = 2
SUBH = SUB // HALVES
BLOCKS = GATES * SUB
BLOCKSH = BLOCKS // HALVES
HIGH_FROM = 8
SPLIT_RNN_AT = 8
WX0_LOADS = 4
CHUNK = 16
GROUP = 8
LAG = 2 * GROUP
Y0_GROUPS = 4
BODY = 2 * CHUNK
CHUNKS = STEPS // CHUNK
GROUPS = STEPS // GROUP
BLOCKS_PER_STEP = BLOCKS // CHUNK
H_SCALE = 2.0 ** 15
CELL = SUB * BATCH
CELLH = CELL // HALVES

fp32, fp16, i32 = mybir.dt.float32, mybir.dt.float16, mybir.dt.int32
ALU = mybir.AluOpType
ACT = mybir.ActivationFunctionType


def residual_lstm_rnn(nc, xT, h0T, wx0, wh0, b0, wx1, wh1, b1, yT):
    with ExitStack() as ctx:
        def sb(name, shape, dt=fp32):
            return ctx.enter_context(nc.sbuf_tensor(name, shape, dt))

        def pb(name):
            return ctx.enter_context(nc.psum_tensor(name, [P, 512], fp32))

        def sem(name):
            return ctx.enter_context(nc.semaphore(name))

        wx0_sb = sb("wx0_sb", [P, WX0_LOADS, SUB, BLOCKS // WX0_LOADS, P])
        wh0_sb = sb("wh0_sb", [P, SUB, BLOCKS, P])
        wx1_sb = sb("wx1_sb", [P, SUB, SUB, P])
        wh1_sb = sb("wh1_sb", [P, SUB, SUB, P])
        wh0_part = [sb(f"wh0_part{i}", [P, SUB, QUADS, BLOCKS * QUAD], fp16) for i in range(2)]
        wh1_part = [sb(f"wh1_part{i}", [P, SUB, SUB * P], fp16) for i in range(2)]
        b0_sb = sb("b0_sb", [P, BLOCKS])
        b1_sb = sb("b1_sb", [P, SUB])
        largest_slice, largest_slice1 = sb("largest_slice", [P, SUB]), sb("largest_slice1", [P, SUB])
        largest = [sb(f"largest{l}", [P, 1]) for l in range(2)]
        largest_all = [sb(f"largest_all{l}", [P, 1]) for l in range(2)]
        power = [sb(f"power{l}", [P, 1]) for l in range(2)]
        w_scale = [sb(f"w_scale{l}", [P, 1]) for l in range(2)]
        w_scale_half = [sb(f"w_scale_half{l}", [P, 1]) for l in range(2)]
        unscale = [sb(f"unscale{l}", [P, 1]) for l in range(2)]
        h_first = sb("h_first", [P, SUB, 2 * BATCH])
        h0_parts = sb("h0_parts", [P, SUB, 2 * BATCH], fp16)
        h1_parts = sb("h1_parts", [P, SUB, 2 * BATCH], fp16)
        x_bulk = sb("x_bulk", [P, 2, SUB, CHUNK * BATCH])
        x_res = sb("x_res", [P, 2, SUB, CHUNK, BATCH])
        xw0 = sb("xw0", [P, 2, CHUNK, BLOCKS * BATCH])
        y0 = sb("y0", [P, Y0_GROUPS, SUB, GROUP, BATCH])
        xw1 = sb("xw1", [P, 2, GROUP, CELL])
        y1 = sb("y1", [P, 2, SUB, GROUP, BATCH])
        turned0 = sb("turned0", [P, BLOCKS, 2 * BATCH])
        sum0 = sb("sum0", [P, HALVES, BLOCKSH * BATCH])
        gates_cell = sb("gates_cell", [P, HALVES, GATES + 1, CELLH])
        uv = sb("uv", [P, HALVES, 2, CELLH])
        o_scaled = sb("o_scaled", [P, HALVES, CELLH])
        h0_full = sb("h0_full", [P, CELL])
        sum1 = sb("sum1", [P, CELL])
        pre1 = sb("pre1", [P, CELL])
        h1_full = sb("h1_full", [P, CELL])

        rec0_ps, rec1_ps = pb("rec0_ps"), pb("rec1_ps")
        bulk0_ps = [pb(f"bulk0_ps{i}") for i in range(2)]
        bulk1_ps = [pb(f"bulk1_ps{i}") for i in range(2)]
        gate_ps = [pb(f"gate_ps{half}") for half in range(HALVES)]
        pre0 = [bank[:, 0:BLOCKSH * BATCH] for bank in gate_ps]
        tanh_c = [bank[:, BLOCKSH * BATCH:BLOCKSH * BATCH + CELLH] for bank in gate_ps]

        wx0_in = [sem(f"wx0_in{m}") for m in range(WX0_LOADS)]
        wh0_in = [sem(f"wh0_in{k}") for k in range(SUB)]
        wh1_in, wx1_in, b_in, h_in = (sem(n) for n in ("wh1_in", "wx1_in", "b_in", "h_in"))
        h_zeroed, cell_zeroed, b0_halved = sem("h_zeroed"), sem("cell_zeroed"), sem("b0_halved")
        prep, largest_done, reduced = sem("prep"), sem("largest_done"), sem("reduced")
        scaled, w_low = sem("scaled"), sem("w_low")
        w_high_act, w_high_pool = sem("w_high_act"), sem("w_high_pool")
        x_bulk_in = [sem(f"x_bulk_in{i}") for i in range(2)]
        x_res_in = [sem(f"x_res_in{i}") for i in range(2)]
        y1_out = [sem(f"y1_out{i}") for i in range(2)]
        def sem_by_half(name):
            return [sem(f"{name}_{half}") for half in range(HALVES)]

        rec0_done = sem("rec0_done")
        turned0_done, sum0_done, pre0_done = (sem_by_half(n) for n in ("turned0_done", "sum0_done", "pre0_done"))
        gates_done, uv_done, cell_done = (sem_by_half(n) for n in ("gates_done", "uv_done", "cell_done"))
        o_scaled_done, tanh_c_done = sem_by_half("o_scaled_done"), sem_by_half("tanh_c_done")
        h0_full_done, h0_ready = sem_by_half("h0_full_done"), sem_by_half("h0_ready")
        y0_done = sem("y0_done")
        bulk0_done, xw0_done = sem("bulk0_done"), sem("xw0_done")
        bulk1_done, xw1_done = sem("bulk1_done"), sem("xw1_done")
        rec1_done, sum1_done, pre1_done = sem("rec1_done"), sem("sum1_done"), sem("pre1_done")
        h1_full_done, h1_high, h1_ready, y1_done = (
            sem("h1_full_done"), sem("h1_high"), sem("h1_ready"), sem("y1_done"))

        def phases(eng, steps):
            steps(0, 0, BODY)
            with eng.Fori(1, STEPS // BODY - 1) as i:
                steps(i, BODY, BODY)
            steps(STEPS // BODY - 1, STEPS - BODY, BODY)
            steps(STEPS // BODY, STEPS, LAG)

        def loads(i, j, ahead):
            return i * 16 + 16 * ((j // CHUNK + ahead) // 2 + 1)

        def is_g(b):
            return b % BLOCKSH // SUBH == GATES - 1

        def w_pieces():
            return ([(0, k, q, lo, hi) for k in range(SUB) for q in range(QUADS) for half in range(0, BLOCKS, BLOCKSH)
                     for lo, hi in ((half, half + BLOCKSH - SUBH), (half + BLOCKSH - SUBH, half + BLOCKSH))]
                    + [(1, k, 0, 0, SUB) for k in range(SUB)])

        def w_piece(l, k, q, lo, hi):
            if l == 1:
                return wh1_sb[:, k].rearrange("p b c -> p (b c)"), wh1_part[0][:, k], wh1_part[1][:, k], w_scale[1][:, :]
            w32 = wh0_sb[:, k, lo:hi, QUAD * q:QUAD * (q + 1)]
            high, low = (h[:, k, q].rearrange("p (b c) -> p b c", c=QUAD)[:, lo:hi] for h in wh0_part)
            return w32, high, low, (w_scale if is_g(lo) else w_scale_half)[0][:, :]

        of_lstm = [p for p in w_pieces() if p[0] == 0]
        of_rnn = [p for p in w_pieces() if p[0] == 1]
        of_lstm_by_act = [p for p in of_lstm if p[2] < QUADS - 1]
        of_lstm_by_pool = [p for p in of_lstm if p[2] == QUADS - 1]


        block = ctx.enter_context(nc.Block())

        @block.sync
        def _(sp):
            sp.dma_start(x_bulk[:, 0], xT[0].rearrange("p s t n -> p s (t n)")).then_inc(x_bulk_in[0], 16)
            sp.dma_start(b0_sb[:, :], b0).then_inc(b_in, 16)
            sp.dma_start(b1_sb[:, :], b1).then_inc(b_in, 16)
            for m, slices_behind in zip(range(WX0_LOADS), ((0, 1), (2, 3), (), ())):
                sp.dma_start(wx0_sb[:, m], wx0[m]).then_inc(wx0_in[m], 16)
                for k in slices_behind:
                    sp.dma_start(wh0_sb[:, k], wh0[:, k]).then_inc(wh0_in[k], 16)
            sp.dma_start(wh1_sb[:, :], wh1).then_inc(wh1_in, 16)
            sp.wait_ge(h_zeroed, 1)
            sp.dma_start(h_first[:, :, 0:BATCH], h0T).then_inc(h_in, 16)
            sp.dma_start(x_res[:, 0], xT[0]).then_inc(x_res_in[0], 16)
            sp.dma_start(x_bulk[:, 1], xT[1].rearrange("p s t n -> p s (t n)")).then_inc(x_bulk_in[1], 16)
            sp.dma_start(wx1_sb[:, :], wx1).then_inc(wx1_in, 16)

            def steps(i, at, count):
                for j in range(0, count, GROUP):
                    t, a = i * BODY + j, at + j
                    v = a // CHUNK
                    if a % CHUNK == 0 and v + 1 < CHUNKS:
                        if a:
                            sp.wait_ge(y0_done, t)
                        chunk = i * (BODY // CHUNK) + j // CHUNK
                        sp.dma_start(x_res[:, (v + 1) % 2], xT[bass.ds(chunk + 1, 1)].rearrange("a p s t n -> (a p) s t n")
                                     ).then_inc(x_res_in[(v + 1) % 2], 16)
                        if v + 2 < CHUNKS:
                            sp.wait_ge(bulk0_done, t * BLOCKS_PER_STEP + BLOCKS)
                            sp.dma_start(x_bulk[:, v % 2], xT[bass.ds(chunk + 2, 1)].rearrange("a p s t n -> (a p) s (t n)")
                                         ).then_inc(x_bulk_in[v % 2], 16)
                    if a >= LAG + GROUP:
                        slot = a // GROUP % 2 ^ 1
                        sp.wait_ge(y1_done, t - LAG)
                        group = i * (BODY // GROUP) + ((j - LAG) // GROUP - 1)
                        sp.dma_start(yT[bass.ds(group, 1)].rearrange("a p s t n -> (a p) s t n"),
                                     y1[:, slot]).then_inc(y1_out[slot], 16)

            phases(sp, steps)
            sp.wait_ge(y1_done, STEPS)
            sp.dma_start(yT[GROUPS - 1], y1[:, 1]).then_inc(y1_out[1], 16)
            for slot in range(2):
                sp.wait_ge(y1_out[slot], 16 * GROUPS // 2)

        @block.gpsimd
        def _(pool):
            nc.gpsimd.memset(h_first[:, :, :], 0.0).then_inc(h_zeroed, 1)
            nc.gpsimd.memset(gates_cell[:, :, GATES], 0.0).then_inc(cell_zeroed, 1)
            for l in range(2):
                if l == 1:
                    pool.wait_ge(scaled, 1)
                    for piece in of_lstm_by_pool:
                        w32, high, low, scale = w_piece(*piece)
                        nc.gpsimd.tensor_scalar(high, w32, scale, None, ALU.mult).then_inc(w_high_pool, 1)
                pool.wait_ge(largest_done, l + 1)
                nc.gpsimd.partition_all_reduce(largest_all[l][:, :], largest[l][:, :], P,
                                               bass.bass_isa.ReduceOp.max).then_inc(reduced, 1)

        @block.tensor
        def _(pe):
            def bulk0(bank, slot, b):
                m, b_m = divmod(b, BLOCKS // WX0_LOADS)
                for k in range(SUB):
                    last = nc.tensor.matmul(bulk0_ps[bank][:, 0:CHUNK * BATCH], wx0_sb[:, m, k, b_m, :], x_bulk[:, slot, k, :],
                                            start=(k == 0), stop=(k == SUB - 1))
                last.then_inc(bulk0_done, 1)

            def keep_clock():
                for _ in range(SUB):
                    nc.tensor.matmul(bulk0_ps[0][:, 0:CHUNK * BATCH], wx0_sb[:, 0, 0, 0, :], x_bulk[:, 0, 0, :],
                                     start=True, stop=True)

            pe.wait_ge(x_bulk_in[0], 16)
            for b in range(BLOCKS):
                if b >= 2:
                    pe.wait_ge(xw0_done, b - 1)
                if b % (BLOCKS // WX0_LOADS) == 0:
                    pe.wait_ge(wx0_in[b // (BLOCKS // WX0_LOADS)], 16)
                bulk0(b % 2, 0, b)

            def recurrent0(states, weights, ready):
                passes = SUB * len(weights)
                for n in range(passes):
                    k, w = divmod(n, len(weights))
                    if w == 0 and k % SUBH == 0:
                        ready(k // SUBH)
                    for q in range(QUADS):
                        last = nc.tensor.matmul(rec0_ps[QUAD * q:QUAD * (q + 1), :], states[:, k, :], weights[w][:, k, q],
                                                start=(n == 0), stop=(n == passes - 1), tile_position=(0, QUAD * q))
                last.then_inc(rec0_done, 1)

            def recurrent1(states, weights, blocks=range(SUB)):
                passes = SUB * len(weights)
                for b in blocks:
                    for n in range(passes):
                        k, w = divmod(n, len(weights))
                        last = nc.tensor.matmul(rec1_ps[:, b * 2 * BATCH:(b + 1) * 2 * BATCH], weights[w][:, k, b * P:(b + 1) * P],
                                                states[:, k, :], start=(n == 0), stop=(n == passes - 1))
                if b == SUB - 1:
                    last.then_inc(rec1_done, 1)

            def steps(i, at, count):
                for j in range(count):
                    t, a = i * BODY + j, at + j
                    if a == 0:
                        pe.wait_ge(h_in, 16)
                        for k in range(SUB):
                            pe.wait_ge(wh0_in[k], 16)
                        recurrent0(h_first, [wh0_sb[:, :, :, :].rearrange("p k b (q c) -> p k q b c", q=QUADS)],
                                   lambda half: None)
                    elif a < STEPS:
                        if a == 1:
                            pe.wait_ge(w_low, 1)
                        recurrent0(h0_parts, wh0_part, lambda half: pe.wait_ge(h0_ready[half], t))
                    v, c = divmod(a, CHUNK)
                    if v + 1 < CHUNKS:
                        if c == 0:
                            pe.wait_ge(x_bulk_in[(v + 1) % 2], loads(i, j, 1))
                        for m in range(BLOCKS_PER_STEP):
                            pe.wait_ge(xw0_done, t * BLOCKS_PER_STEP + (BLOCKS + m - 1))
                            bulk0((c * BLOCKS_PER_STEP + m) % 2, (v + 1) % 2, c * BLOCKS_PER_STEP + m)
                    elif a < STEPS:
                        if c == 0:
                            pe.wait_ge(xw0_done, t * BLOCKS_PER_STEP + BLOCKS)
                        keep_clock()
                    if GROUP <= a < STEPS + GROUP:
                        g8, slot = a % GROUP, (a // GROUP - 1) % Y0_GROUPS
                        b, half = divmod(g8, GROUP // SUB)
                        if a == GROUP:
                            pe.wait_ge(wx1_in, 16)
                        if g8 == 0:
                            pe.wait_ge(y0_done, t)
                        if half == 0 and a >= GROUP + 4:
                            pe.wait_ge(xw1_done, t - (GROUP + 2))
                        for k in range(2 * half, 2 * half + 2):
                            last = nc.tensor.matmul(bulk1_ps[b % 2][:, 0:GROUP * BATCH], wx1_sb[:, k, b, :],
                                                    y0[:, slot, k].rearrange("p t n -> p (t n)"),
                                                    start=(k == 0), stop=(k == SUB - 1))
                        last.then_inc(bulk1_done, 1)
                    if LAG - SUB <= a < LAG:
                        if a == LAG - SUB:
                            pe.wait_ge(wh1_in, 16)
                        recurrent1(h_first, [wh1_sb[:, :].rearrange("p k b c -> p k (b c)")], (a - (LAG - SUB),))
                    elif a > LAG:
                        if a == LAG + 1:
                            pe.wait_ge(w_low, 2)
                        pe.wait_ge(h1_ready, t - LAG)
                        recurrent1(h1_parts, wh1_part)

            phases(pe, steps)

        @block.vector
        def _(dve):
            dve.wait_ge(b_in, 32)
            halved = b0_sb[:, :].rearrange("p (h b) -> p h b", h=HALVES)[:, :, 0:BLOCKSH - SUBH]
            nc.vector.tensor_scalar(halved, halved, 0.5, None, ALU.mult).then_inc(b0_halved, 1)
            def abs_max(out, in_):
                return nc.vector.tensor_reduce(out, in_, mybir.AxisListType.X, ALU.max, apply_absolute_value=True)

            for k in range(SUB):
                dve.wait_ge(wh0_in[k], 16)
                last = abs_max(largest_slice[:, k:k + 1], wh0_sb[:, k].rearrange("p b c -> p (b c)"))
            last.then_inc(prep, 1)
            dve.wait_ge(prep, 1)
            abs_max(largest[0][:, :], largest_slice[:, :]).then_inc(largest_done, 1)

            def find_scale(l, done):
                dve.wait_ge(reduced, l + 1)
                nc.vector.tensor_scalar(largest_all[l][:, :], largest_all[l][:, :], 2.0 ** -100, None,
                                        ALU.max).then_inc(prep, 1)
                dve.wait_ge(prep, done + 1)
                nc.vector.tensor_scalar(power[l][:, :].bitcast(i32), largest_all[l][:, :].bitcast(i32), 0x7F800000, None,
                                        ALU.bitwise_and).then_inc(prep, 1)
                dve.wait_ge(prep, done + 2)
                nc.vector.tensor_scalar(w_scale[l][:, :].bitcast(i32), power[l][:, :].bitcast(i32), -1.0,
                                        float((2 * 127 + 14) << 23), ALU.mult, ALU.add).then_inc(prep, 1)
                dve.wait_ge(prep, done + 3)
                nc.vector.tensor_scalar(w_scale_half[l][:, :], w_scale[l][:, :], 0.5, None, ALU.mult).then_inc(prep, 1)
                nc.vector.tensor_scalar(unscale[l][:, :], power[l][:, :], 2.0 ** -14 / H_SCALE, None,
                                        ALU.mult).then_inc(scaled, 1)
                dve.wait_ge(scaled, l + 1)
                return done + 4

            def low_part(piece, high_done, n):
                w32, high, low, scale = w_piece(*piece)
                dve.wait_ge(high_done, n)
                return nc.vector.scalar_tensor_tensor(low, w32, scale, high, ALU.mult, ALU.subtract)

            done = find_scale(0, 1)
            for piece in of_lstm:
                if piece in of_lstm_by_act:
                    last = low_part(piece, w_high_act, of_lstm_by_act.index(piece) + 1)
                else:
                    last = low_part(piece, w_high_pool, of_lstm_by_pool.index(piece) + 1)
            last.then_inc(w_low, 1)

            def split_rnn_weights(a):
                if 1 <= a <= SUB:
                    if a == 1:
                        dve.wait_ge(wh1_in, 16)
                    last = abs_max(largest_slice1[:, a - 1:a], wh1_sb[:, a - 1].rearrange("p b c -> p (b c)"))
                    if a == SUB:
                        last.then_inc(prep, 1)
                elif a == SUB + 1:
                    dve.wait_ge(prep, done + 1)
                    abs_max(largest[1][:, :], largest_slice1[:, :]).then_inc(largest_done, 1)
                elif a == SUB + 3:
                    find_scale(1, done + 1)
                elif SPLIT_RNN_AT < a <= SPLIT_RNN_AT + SUB:
                    n = a - SPLIT_RNN_AT - 1
                    last = low_part(of_rnn[n], w_high_act, len(of_lstm_by_act) + n + 1)
                    if n == SUB - 1:
                        last.then_inc(w_low, 1)

            def slices(ap):
                return ap.rearrange("p (s n) -> p s n", n=BATCH)

            all_blocks, first_blocks, last_blocks = (0, BLOCKSH), (0, BLOCKSH // 2), (BLOCKSH // 2, BLOCKSH)
            first_quarter, second_quarter = (0, BLOCKSH // 4), (BLOCKSH // 4, BLOCKSH // 2)

            def turn0(half, part):
                lo, hi = half * BLOCKSH + part[0], half * BLOCKSH + part[1]
                return nc.vector.transpose(turned0[:, lo:hi].rearrange("p b n -> p (b n)"), rec0_ps[:, lo * QUAD:hi * QUAD])

            def add_parts0(half, part, n):
                dve.wait_ge(turned0_done[half], n)
                blocks = turned0[:, half * BLOCKSH + part[0]:half * BLOCKSH + part[1]]
                nc.vector.tensor_tensor(slices(sum0[:, half, part[0] * BATCH:part[1] * BATCH]), blocks[:, :, 0:BATCH],
                                        blocks[:, :, BATCH:], ALU.add).then_inc(sum0_done[half], 1)

            def add_xw0(half, n, a):
                dve.wait_ge(sum0_done[half], (half + 1) * n)
                cols = slice(half * BLOCKSH * BATCH, (half + 1) * BLOCKSH * BATCH)
                xw = xw0[:, a // CHUNK % 2, a % CHUNK, cols]
                if a:
                    nc.vector.scalar_tensor_tensor(pre0[half], sum0[:, half], unscale[0][:, :], xw,
                                                   ALU.mult, ALU.add).then_inc(pre0_done[half], 1)
                else:
                    sig = (GATES - 1) * CELLH
                    nc.vector.scalar_tensor_tensor(pre0[half][:, 0:sig], sum0[:, half, 0:sig], 0.5, xw[:, 0:sig],
                                                   ALU.mult, ALU.add)
                    nc.vector.tensor_tensor(pre0[half][:, sig:], sum0[:, half, sig:], xw[:, sig:],
                                            ALU.add).then_inc(pre0_done[half], 1)

            def gate_products(half, n):
                dve.wait_ge(gates_done[half], n)
                nc.vector.scalar_tensor_tensor(uv[:, half], gates_cell[:, half, 0:2], 1.0, gates_cell[:, half, 3:5],
                                               ALU.add, ALU.mult).then_inc(uv_done[half], 1)

            def cell(half, n):
                dve.wait_ge(uv_done[half], n)
                nc.vector.scalar_tensor_tensor(gates_cell[:, half, GATES], uv[:, half, 1], 0.5, uv[:, half, 0],
                                               ALU.mult, ALU.add).then_inc(cell_done[half], 1)

            def state_cols(half):
                return slice(half * CELLH, (half + 1) * CELLH), slice(half * SUBH, (half + 1) * SUBH)

            def state_high(half, n):
                cols, subs = state_cols(half)
                dve.wait_ge(o_scaled_done[half], n)
                dve.wait_ge(tanh_c_done[half], n)
                nc.vector.tensor_tensor(h0_parts[:, subs, 0:BATCH], slices(o_scaled[:, half]), slices(tanh_c[half]), ALU.mult)
                nc.vector.tensor_tensor(h0_full[:, cols], o_scaled[:, half], tanh_c[half],
                                        ALU.mult).then_inc(h0_full_done[half], 1)

            def state_low(half, n):
                cols, subs = state_cols(half)
                dve.wait_ge(h0_full_done[half], n)
                nc.vector.tensor_tensor(h0_parts[:, subs, BATCH:], slices(h0_full[:, cols]), h0_parts[:, subs, 0:BATCH],
                                        ALU.subtract).then_inc(h0_ready[half], 1)

            def product1():
                return rec1_ps[:, 0:SUB * 2 * BATCH].rearrange("p (b n) -> p b n", n=2 * BATCH)

            def scale1(s_a):
                return unscale[1][:, :] if s_a else 1.0

            def add_low1(s_n, s_a):
                if s_a % GROUP == 0:
                    dve.wait_ge(xw1_done, s_n + (GROUP - 1))
                dve.wait_ge(rec1_done, s_n)
                nc.vector.scalar_tensor_tensor(slices(sum1[:, :]), product1()[:, :, BATCH:], scale1(s_a),
                                               slices(xw1[:, s_a // GROUP % 2, s_a % GROUP]),
                                               ALU.mult, ALU.add).then_inc(sum1_done, 1)

            def add_high1(s_n, s_a):
                dve.wait_ge(sum1_done, s_n)
                nc.vector.scalar_tensor_tensor(slices(pre1[:, :]), product1()[:, :, 0:BATCH], scale1(s_a), slices(sum1[:, :]),
                                               ALU.mult, ALU.add).then_inc(pre1_done, 1)

            def state1_high(s_n):
                dve.wait_ge(h1_full_done, s_n)
                nc.vector.tensor_scalar(h1_parts[:, :, 0:BATCH], slices(h1_full[:, :]), H_SCALE, None,
                                        ALU.mult).then_inc(h1_high, 1)

            def state1_low(s_n):
                dve.wait_ge(h1_high, s_n)
                nc.vector.scalar_tensor_tensor(h1_parts[:, :, BATCH:], slices(h1_full[:, :]), H_SCALE, h1_parts[:, :, 0:BATCH],
                                               ALU.mult, ALU.subtract).then_inc(h1_ready, 1)

            def add_y1(s_a, stored):
                slot = s_a // GROUP % 2
                if s_a % GROUP == 0 and s_a >= 2 * GROUP:
                    dve.wait_ge(y1_out[slot], stored)
                nc.vector.tensor_tensor(y1[:, slot, :, s_a % GROUP], y0[:, s_a // GROUP % Y0_GROUPS, :, s_a % GROUP],
                                        slices(h1_full[:, :]), ALU.add).then_inc(y1_done, 1)

            def add_y0(t, a, loaded):
                v = a // CHUNK
                if a % CHUNK == 0:
                    dve.wait_ge(x_res_in[v % 2], loaded)
                if a % GROUP == 0 and a >= Y0_GROUPS * GROUP:
                    dve.wait_ge(bulk1_done, t - (Y0_GROUPS - 1) * GROUP)
                nc.vector.scalar_tensor_tensor(y0[:, a // GROUP % Y0_GROUPS, :, a % GROUP], slices(h0_full[:, :]), 1.0 / H_SCALE,
                                               x_res[:, v % 2, :, a % CHUNK], ALU.mult, ALU.add).then_inc(y0_done, 1)

            def steps(i, at, count):
                for j in range(count):
                    t, a = i * BODY + j, at + j
                    n = t + 1
                    s_a, s_n = a - LAG, t - (LAG - 1)
                    stored = i * (16 * BODY // (2 * GROUP)) + 16 * ((j - LAG) // GROUP // 2)
                    lstm, rnn = a < STEPS, a >= LAG
                    if lstm:
                        if a % CHUNK == 0:
                            dve.wait_ge(xw0_done, t * BLOCKS_PER_STEP + BLOCKS)
                        dve.wait_ge(rec0_done, n)
                        if a == 0:
                            dve.wait_ge(cell_zeroed, 1)
                        turn0(0, all_blocks).then_inc(turned0_done[0], 1)
                        turn0(1, first_quarter)
                        add_parts0(0, all_blocks, n)
                        turn0(1, second_quarter).then_inc(turned0_done[1], 1)
                        add_xw0(0, n, a)
                        turn0(1, last_blocks).then_inc(turned0_done[1], 1)
                        add_parts0(1, first_blocks, 2 * n - 1)
                        gate_products(0, n)
                        add_parts0(1, last_blocks, 2 * n)
                        cell(0, n)
                        add_xw0(1, n, a)
                        state_high(0, n)
                        gate_products(1, n)
                        state_low(0, n)
                        cell(1, n)
                    if rnn:
                        add_low1(s_n, s_a)
                    if lstm:
                        state_high(1, n)
                        state_low(1, n)
                    if rnn:
                        add_high1(s_n, s_a)
                    if lstm:
                        add_y0(t, a, loads(i, j, 0))
                        split_rnn_weights(a)
                    if rnn:
                        state1_high(s_n)
                        add_y1(s_a, stored)
                        state1_low(s_n)

            phases(dve, steps)

        @block.scalar
        def _(act):
            def evacuate0(bank, slot, b):
                out = xw0[:, slot, :, b * BATCH:(b + 1) * BATCH]
                nc.scalar.activation(out, bulk0_ps[bank][:, 0:CHUNK * BATCH].rearrange("p (t n) -> p t n", n=BATCH),
                                     ACT.Identity, bias=b0_sb[:, b:b + 1],
                                     scale=1.0 if is_g(b) else 0.5).then_inc(xw0_done, 1)

            def high_parts(pieces):
                for piece in pieces:
                    w32, high, low, scale = w_piece(*piece)
                    nc.scalar.activation(high, w32, ACT.Copy, scale=scale).then_inc(w_high_act, 1)

            act.wait_ge(b0_halved, 1)
            share = len(of_lstm_by_act) // (BLOCKS - HIGH_FROM)
            for b in range(BLOCKS):
                if b == HIGH_FROM:
                    act.wait_ge(scaled, 1)
                if b >= HIGH_FROM:
                    at = (b - HIGH_FROM) * share
                    high_parts(of_lstm_by_act[at:at + share] if b < BLOCKS - 1 else of_lstm_by_act[at:])
                act.wait_ge(bulk0_done, b + 1)
                evacuate0(b % 2, 0, b)

            def steps(i, at, count):
                for j in range(count):
                    t, a = i * BODY + j, at + j
                    if a < STEPS:
                        for half in range(HALVES):
                            act.wait_ge(pre0_done[half], t + 1)
                            nc.scalar.activation(gates_cell[:, half, 0:GATES].rearrange("p g n -> p (g n)"), pre0[half],
                                                 ACT.Tanh).then_inc(gates_done[half], 1)
                            act.wait_ge(gates_done[half], t + 1)
                            nc.scalar.activation(o_scaled[:, half], gates_cell[:, half, 2], ACT.Copy, bias=H_SCALE / 2,
                                                 scale=H_SCALE / 2).then_inc(o_scaled_done[half], 1)
                            act.wait_ge(cell_done[half], t + 1)
                            nc.scalar.activation(tanh_c[half], gates_cell[:, half, GATES], ACT.Tanh,
                                                 scale=0.5).then_inc(tanh_c_done[half], 1)
                    if SPLIT_RNN_AT <= a < SPLIT_RNN_AT + SUB:
                        act.wait_ge(scaled, 2)
                        high_parts(of_rnn[a - SPLIT_RNN_AT:a - SPLIT_RNN_AT + 1])
                    v, c = divmod(a, CHUNK)
                    if v + 1 < CHUNKS:
                        for m in range(BLOCKS_PER_STEP):
                            b = c * BLOCKS_PER_STEP + m
                            act.wait_ge(bulk0_done, t * BLOCKS_PER_STEP + (BLOCKS + m + 1))
                            evacuate0(b % 2, (v + 1) % 2, b)
                    if GROUP <= a < STEPS + GROUP and a % 2:
                        b, slot = a % GROUP // 2, a // GROUP % 2 ^ 1
                        act.wait_ge(bulk1_done, t - (GROUP - 1))
                        nc.scalar.activation(xw1[:, slot, :, b * BATCH:(b + 1) * BATCH],
                                             bulk1_ps[b % 2][:, 0:GROUP * BATCH].rearrange("p (t n) -> p t n", n=BATCH),
                                             ACT.Identity, bias=b1_sb[:, b:b + 1], scale=1.0).then_inc(xw1_done, 2)
                    if a >= LAG:
                        act.wait_ge(pre1_done, t - (LAG - 1))
                        nc.scalar.activation(h1_full[:, :], pre1[:, :], ACT.Tanh).then_inc(h1_full_done, 1)

            phases(act, steps)


def kernel(x, cond_1024, L0_cond_Wx, L0_cond_Wh, L0_cond_b, L1_cond_Wx, L1_cond_Wh, L1_cond_b):
    import concourse.bacc as bacc
    from concourse.bass_utils import run_bass_kernel_spmd

    def laid(a, shape, order):
        return np.ascontiguousarray(np.asarray(a).reshape(shape).transpose(order))

    def gates(a):
        a = np.asarray(a)
        return a.reshape(*a.shape[:-1], GATES, HALVES, SUBH * P).swapaxes(-3, -2).reshape(a.shape)

    arrays = {
        "xT": laid(x, (BATCH, CHUNKS, CHUNK, SUB, P), (1, 4, 3, 2, 0)),
        "h0T": laid(cond_1024, (BATCH, SUB, P), (2, 1, 0)),
        "wx0": laid(gates(L0_cond_Wx), (SUB, P, WX0_LOADS, BLOCKS // WX0_LOADS, P), (2, 1, 0, 3, 4)),
        "wh0": laid(gates(L0_cond_Wh), (SUB, P, BLOCKS, P), (1, 0, 2, 3)),
        "b0": laid(gates(L0_cond_b), (BLOCKS, P), (1, 0)),
        "wx1": laid(L1_cond_Wx, (SUB, P, SUB, P), (1, 0, 2, 3)),
        "wh1": laid(L1_cond_Wh, (SUB, P, SUB, P), (1, 0, 2, 3)),
        "b1": laid(L1_cond_b, (SUB, P), (1, 0)),
    }
    nc = bacc.Bacc("TRN2", target_bir_lowering=False, num_devices=1)
    args = [nc.dram_tensor(n, a.shape, mybir.dt.from_np(a.dtype), kind="ExternalInput").ap() for n, a in arrays.items()]
    out = nc.dram_tensor("yT", (GROUPS, P, SUB, GROUP, BATCH), fp32, kind="ExternalOutput").ap()
    residual_lstm_rnn(nc, *args, out)
    r = run_bass_kernel_spmd(nc, [arrays], core_ids=[0])
    y = np.asarray(r.results[0]["yT"])
    return np.ascontiguousarray(y.transpose(4, 0, 3, 2, 1)).reshape(BATCH, STEPS, DIM)
```
